# Optimizing a Trainium2 kernel written in Bass

```python
import numpy as np
import jax
import jax.numpy as jnp

def _softmax(x, axis=-1):
    return jax.nn.softmax(x, axis=axis)

def _gelu(x):
    return jax.nn.gelu(x, approximate=True)

def _silu(x):
    return jax.nn.silu(x)

def _sigmoid(x):
    return jax.nn.sigmoid(x)

def _layernorm(x, axis=-1, eps=1e-05):
    m = jnp.mean(x, axis=axis, keepdims=True)
    v = jnp.var(x, axis=axis, keepdims=True)
    return (x - m) / jnp.sqrt(v + eps)

def _scatter_add(tgt, idx, src, axis=0):
    return tgt.at[idx].add(src)

def _segment_sum(src, seg, n):
    return jax.ops.segment_sum(src, seg, n)
kernel_name = 'mk_dlrm_tower_d1_rec_r8_ea749c'

def setup_inputs(seed: int=0):
    np.random.seed(seed)
    _w = jnp.asarray

    def _rec_inputs():
        import jax
        import jax.numpy as jnp
        _tk = jax.random.key(seed)
        ids = jnp.stack([jax.random.randint(jax.random.fold_in(_tk, 200 + f), (512,), 0, v, jnp.int32) for f, v in enumerate([125000, 1000, 12500, 1250, 1250, 1250, 12500, 1000, 1000, 12500, 12500, 1250, 1000, 12500, 12500, 1000, 1250, 1250, 1000, 1000, 12500, 1250, 1000, 12500, 1000, 1250])], axis=1)
        tbl_0 = 0.05 * jax.random.normal(jax.random.fold_in(_tk, 500 + 0), (125000, 128), jnp.float32)
        tbl_1 = 0.05 * jax.random.normal(jax.random.fold_in(_tk, 500 + 1), (1000, 128), jnp.float32)
        tbl_2 = 0.05 * jax.random.normal(jax.random.fold_in(_tk, 500 + 2), (12500, 128), jnp.float32)
        tbl_3 = 0.05 * jax.random.normal(jax.random.fold_in(_tk, 500 + 3), (1250, 128), jnp.float32)
        tbl_4 = 0.05 * jax.random.normal(jax.random.fold_in(_tk, 500 + 4), (1250, 128), jnp.float32)
        tbl_5 = 0.05 * jax.random.normal(jax.random.fold_in(_tk, 500 + 5), (1250, 128), jnp.float32)
        tbl_6 = 0.05 * jax.random.normal(jax.random.fold_in(_tk, 500 + 6), (12500, 128), jnp.float32)
        tbl_7 = 0.05 * jax.random.normal(jax.random.fold_in(_tk, 500 + 7), (1000, 128), jnp.float32)
        tbl_8 = 0.05 * jax.random.normal(jax.random.fold_in(_tk, 500 + 8), (1000, 128), jnp.float32)
        tbl_9 = 0.05 * jax.random.normal(jax.random.fold_in(_tk, 500 + 9), (12500, 128), jnp.float32)
        tbl_10 = 0.05 * jax.random.normal(jax.random.fold_in(_tk, 500 + 10), (12500, 128), jnp.float32)
        tbl_11 = 0.05 * jax.random.normal(jax.random.fold_in(_tk, 500 + 11), (1250, 128), jnp.float32)
        tbl_12 = 0.05 * jax.random.normal(jax.random.fold_in(_tk, 500 + 12), (1000, 128), jnp.float32)
        tbl_13 = 0.05 * jax.random.normal(jax.random.fold_in(_tk, 500 + 13), (12500, 128), jnp.float32)
        tbl_14 = 0.05 * jax.random.normal(jax.random.fold_in(_tk, 500 + 14), (12500, 128), jnp.float32)
        tbl_15 = 0.05 * jax.random.normal(jax.random.fold_in(_tk, 500 + 15), (1000, 128), jnp.float32)
        tbl_16 = 0.05 * jax.random.normal(jax.random.fold_in(_tk, 500 + 16), (1250, 128), jnp.float32)
        tbl_17 = 0.05 * jax.random.normal(jax.random.fold_in(_tk, 500 + 17), (1250, 128), jnp.float32)
        tbl_18 = 0.05 * jax.random.normal(jax.random.fold_in(_tk, 500 + 18), (1000, 128), jnp.float32)
        tbl_19 = 0.05 * jax.random.normal(jax.random.fold_in(_tk, 500 + 19), (1000, 128), jnp.float32)
        tbl_20 = 0.05 * jax.random.normal(jax.random.fold_in(_tk, 500 + 20), (12500, 128), jnp.float32)
        tbl_21 = 0.05 * jax.random.normal(jax.random.fold_in(_tk, 500 + 21), (1250, 128), jnp.float32)
        tbl_22 = 0.05 * jax.random.normal(jax.random.fold_in(_tk, 500 + 22), (1000, 128), jnp.float32)
        tbl_23 = 0.05 * jax.random.normal(jax.random.fold_in(_tk, 500 + 23), (12500, 128), jnp.float32)
        tbl_24 = 0.05 * jax.random.normal(jax.random.fold_in(_tk, 500 + 24), (1000, 128), jnp.float32)
        tbl_25 = 0.05 * jax.random.normal(jax.random.fold_in(_tk, 500 + 25), (1250, 128), jnp.float32)
        _rk = jax.random.fold_in(_tk, 7)
        r_dense_output = -0.000520686 + 1.00062 * jax.random.normal(jax.random.fold_in(_rk, 101), (512, 128), jnp.float32)
        W_top1 = 0.0405887 * jax.random.normal(jax.random.fold_in(_tk, 801), (607, 512), jnp.float32)
        W_top2 = 0.0441942 * jax.random.normal(jax.random.fold_in(_tk, 802), (512, 256), jnp.float32)
        W_top3 = 0.0625 * jax.random.normal(jax.random.fold_in(_tk, 803), (256, 1), jnp.float32)
        b_top1 = jnp.zeros((512,), jnp.float32)
        b_top2 = jnp.zeros((256,), jnp.float32)
        return (r_dense_output, ids, tbl_0, tbl_1, tbl_2, tbl_3, tbl_4, tbl_5, tbl_6, tbl_7, tbl_8, tbl_9, tbl_10, tbl_11, tbl_12, tbl_13, tbl_14, tbl_15, tbl_16, tbl_17, tbl_18, tbl_19, tbl_20, tbl_21, tbl_22, tbl_23, tbl_24, tbl_25, W_top1, b_top1, W_top2, b_top2, W_top3)
    r_dense_output, ids, tbl_0, tbl_1, tbl_2, tbl_3, tbl_4, tbl_5, tbl_6, tbl_7, tbl_8, tbl_9, tbl_10, tbl_11, tbl_12, tbl_13, tbl_14, tbl_15, tbl_16, tbl_17, tbl_18, tbl_19, tbl_20, tbl_21, tbl_22, tbl_23, tbl_24, tbl_25, W_top1, b_top1, W_top2, b_top2, W_top3 = _rec_inputs()

    def _L0_rec_setup():
        import jax, jax.numpy as jnp
        import numpy as np
        B, NUM_SPARSE, D = (2048, 26, 128)
        key = jax.random.key(seed)
        k1, k2 = jax.random.split(key)
        dense_output = jax.random.normal(k1, (B, D), dtype=jnp.float32)
        embeddings = jax.random.normal(k2, (B, NUM_SPARSE, D), dtype=jnp.float32)
        return {'dense_output': dense_output, 'embeddings': embeddings}
    _L0_rec_all = _L0_rec_setup()
    _L0_rec_in = {k: v for k, v in _L0_rec_all.items() if k in ()}
    del _L0_rec_all
    return {'r_dense_output': r_dense_output, 'ids': ids, 'tbl_0': tbl_0, 'tbl_1': tbl_1, 'tbl_2': tbl_2, 'tbl_3': tbl_3, 'tbl_4': tbl_4, 'tbl_5': tbl_5, 'tbl_6': tbl_6, 'tbl_7': tbl_7, 'tbl_8': tbl_8, 'tbl_9': tbl_9, 'tbl_10': tbl_10, 'tbl_11': tbl_11, 'tbl_12': tbl_12, 'tbl_13': tbl_13, 'tbl_14': tbl_14, 'tbl_15': tbl_15, 'tbl_16': tbl_16, 'tbl_17': tbl_17, 'tbl_18': tbl_18, 'tbl_19': tbl_19, 'tbl_20': tbl_20, 'tbl_21': tbl_21, 'tbl_22': tbl_22, 'tbl_23': tbl_23, 'tbl_24': tbl_24, 'tbl_25': tbl_25, 'W_top1': W_top1, 'b_top1': b_top1, 'W_top2': W_top2, 'b_top2': b_top2, 'W_top3': W_top3}

def reference(r_dense_output, ids, tbl_0, tbl_1, tbl_2, tbl_3, tbl_4, tbl_5, tbl_6, tbl_7, tbl_8, tbl_9, tbl_10, tbl_11, tbl_12, tbl_13, tbl_14, tbl_15, tbl_16, tbl_17, tbl_18, tbl_19, tbl_20, tbl_21, tbl_22, tbl_23, tbl_24, tbl_25, W_top1, b_top1, W_top2, b_top2, W_top3):
    import jax
    import jax.numpy as jnp

    def _L0_rec_ref(dense_output, embeddings):
        import jax, jax.numpy as jnp
        import numpy as np
        B, NUM_SPARSE, D = (2048, 26, 128)
        combined = jnp.concatenate([dense_output[:, None, :], embeddings], axis=1)
        interactions = jnp.einsum('bfd,bgd->bfg', combined, combined)
        F = combined.shape[1]
        iu, ju = jnp.triu_indices(F, k=1)
        interactions_flat = interactions[:, iu, ju]
        return jnp.concatenate([dense_output, interactions_flat], axis=1)
    e = jnp.stack([tbl_0[ids[:, 0]], tbl_1[ids[:, 1]], tbl_2[ids[:, 2]], tbl_3[ids[:, 3]], tbl_4[ids[:, 4]], tbl_5[ids[:, 5]], tbl_6[ids[:, 6]], tbl_7[ids[:, 7]], tbl_8[ids[:, 8]], tbl_9[ids[:, 9]], tbl_10[ids[:, 10]], tbl_11[ids[:, 11]], tbl_12[ids[:, 12]], tbl_13[ids[:, 13]], tbl_14[ids[:, 14]], tbl_15[ids[:, 15]], tbl_16[ids[:, 16]], tbl_17[ids[:, 17]], tbl_18[ids[:, 18]], tbl_19[ids[:, 19]], tbl_20[ids[:, 20]], tbl_21[ids[:, 21]], tbl_22[ids[:, 22]], tbl_23[ids[:, 23]], tbl_24[ids[:, 24]], tbl_25[ids[:, 25]]], axis=1)
    z = _L0_rec_ref(r_dense_output, e)
    z = z.reshape(z.shape[0], -1)
    h = jnp.concatenate([z, r_dense_output], axis=1)
    h = jnp.maximum(h @ W_top1 + b_top1, 0.0)
    h = jnp.maximum(h @ W_top2 + b_top2, 0.0)
    y = h @ W_top3
    return y

_drawn_inputs = setup_inputs


def setup_inputs(seed=0):
    import zlib

    import numpy as np

    out = dict(_drawn_inputs(seed))
    spreads = {'b_top1': (0.0, 0.1), 'b_top2': (0.0, 0.1)}
    factors = {}
    for name, (base, spread) in spreads.items():
        noise = np.random.default_rng([zlib.crc32(name.encode()), seed]).standard_normal(out[name].shape)
        drawn = base * np.exp(spread * noise) if base else spread * noise
        out[name] = jnp.asarray(drawn.astype(out[name].dtype))
    for name, factor in factors.items():
        out[name] = (out[name] * factor).astype(out[name].dtype)
    return out
```

```python
from contextlib import ExitStack

import concourse.bass as bass
import numpy as np
from concourse import mybir

F32 = mybir.dt.float32
F32R = mybir.dt.float32r
I32 = mybir.dt.int32
ALU = mybir.AluOpType
ACT = mybir.ActivationFunctionType

P = 128
BATCH = 512
D = 128
TABLES = 26
NEURONS_1 = 512
NEURONS_2 = 256
ROWS = [125000, 1000, 12500, 1250, 1250, 1250, 12500, 1000, 1000, 12500, 12500, 1250, 1000,
        12500, 12500, 1000, 1250, 1250, 1000, 1000, 12500, 1250, 1000, 12500, 1000, 1250]

ONEHOT_ROWS = 1000
CHUNK_ROWS = 125
CHUNKS = ONEHOT_ROWS // CHUNK_ROWS
ONEHOT = [f for f in range(TABLES) if ROWS[f] == ONEHOT_ROWS][:8]
GATHERED = [f for f in range(TABLES) if f not in ONEHOT]
ROUNDS_A = len(ONEHOT) // 2
DVE_CHUNKS = 6
ACT_CHUNKS = CHUNKS - DVE_CHUNKS
TABLE_CUT = 112

TILES = BATCH // P
ROUNDS_B = TILES // 2

FIXED = 1 + len(ONEHOT)
SLOTS = 1 + TABLES
STRIP = 32
HALF = SLOTS // 2
BLOCKS = HALF + 1
KTILES = 4
BLOCKS_OF_STRIP = [len(range(q, BLOCKS, 4)) for q in range(4)]

GROUPS = [GATHERED[i:i + 4] for i in range(0, len(GATHERED), 4)]
EARLY_GROUPS = 2

UNITS = 4
PER_BANK = 16
NT_1 = NEURONS_1 // P
NT_2 = NEURONS_2 // P


def feature_of_slot():
    return [0] + [1 + f for f in ONEHOT] + [1 + f for f in GATHERED]


def dense_places():
    free = []
    for kt in range(KTILES):
        for q in range(4):
            first = SLOTS if 4 * kt + q < BLOCKS else 0
            free += [(kt, STRIP * q + r) for r in range(first, STRIP)]
    return free[:D]


def pair_places():
    feature = feature_of_slot()
    places = []
    for i in range(BLOCKS):
        kt, q = divmod(i, 4)
        for r in range(SLOTS):
            if i + 1 <= r <= i + HALF:
                if i < HALF:
                    places.append((kt, STRIP * q + r, feature[r], feature[i], True))
            elif r != i:
                places.append((kt, STRIP * q + r, feature[r], feature[i + HALF], False))
    assert len({frozenset(x[2:4]) for x in places}) == len(places) == SLOTS * (SLOTS - 1) // 2
    return places


def tower(nc, ids_gathered, ids_onehot, small_tables, tables, dense_t, dense_rows, w1_first, w1_second,
          w2, consts, params, pair_mask, out):
    with ExitStack() as ctx:
        def sb(name, shape, dt=F32):
            return ctx.enter_context(nc.sbuf_tensor(name, shape, dt))

        def psum(name, shape):
            return ctx.enter_context(nc.psum_tensor(name, shape, F32))

        def sem(name):
            return ctx.enter_context(nc.semaphore(name))

        def sem2(name):
            return [sem(f"{name}_{b}") for b in "ab"]

        ids_all = sb("ids_all", [P, TILES * len(GATHERED)], I32)
        ids_now = sb("ids_now", [P, 2, len(GATHERED)], I32)
        rows = sb("rows", [P, 2, len(GATHERED), D])
        table_raw = sb("table_raw", [CHUNK_ROWS, 2, CHUNKS, D])
        table_hi = sb("table_hi", [CHUNK_ROWS, 2, CHUNKS, D], F32R)
        table_lo = sb("table_lo", [CHUNK_ROWS, 2, CHUNKS, D], F32R)
        ids_bc = sb("ids_bc", [CHUNK_ROWS, 2, BATCH], I32)
        distance = sb("distance", [CHUNK_ROWS, 2, ACT_CHUNKS, BATCH])
        onehot = [sb(f"onehot_{b}", [CHUNK_ROWS, CHUNKS, BATCH], F32R) for b in "ab"]
        fixed_t = sb("fixed_t", [P, FIXED, BATCH])
        feats = [sb(f"feats_{b}", [P, P * SLOTS]) for b in "ab"]
        z = [sb(f"z_{b}", [P, KTILES, P]) for b in "ab"]
        w1 = sb("w1", [P, KTILES, NEURONS_1])
        w1_more = sb("w1_more", [P, KTILES, NEURONS_1])
        w2_sb = sb("w2_sb", [P, NT_1, NEURONS_2])
        const_sb = sb("const_sb", [P, P + 2 * CHUNKS])
        param_sb = sb("param_sb", [P, NT_1 + 2 * NT_2])
        mask_sb = sb("mask_sb", [P, KTILES], I32)
        h1 = sb("h1", [P, NT_1, P])
        h2 = sb("h2", [P, NT_2, P])
        y_row = sb("y_row", [1, BATCH])

        identity = const_sb[:, 0:P]
        row_id = const_sb[0:CHUNK_ROWS, P:P + CHUNKS]
        minus_row_id = const_sb[0:CHUNK_ROWS, P + CHUNKS:P + 2 * CHUNKS]
        b1_sb = param_sb[:, 0:NT_1]
        b2_sb = param_sb[:, NT_1:NT_1 + NT_2]
        w3_sb = param_sb[:, NT_1 + NT_2:NT_1 + 2 * NT_2]

        gram = psum("gram", [P, 4, 512])
        turned = [psum(f"turned_{i}", [P, 4, P]) for i in range(2)]
        layer2 = [psum(f"layer2_{i}", [P, 512]) for i in range(2)]

        ids_loaded = sem("ids_loaded")
        consts_loaded = sem("consts_loaded")
        dense_loaded = sem("dense_loaded")
        w1_loaded = sem("w1_loaded")
        params_loaded = sem("params_loaded")
        w1_summed = sem("w1_summed")
        table_loaded = sem2("table_loaded")
        ids_bc_loaded = sem2("ids_bc_loaded")
        hi_done = sem2("hi_done")
        lo_done = sem2("lo_done")
        dve_onehot = sem2("dve_onehot")
        act_distance = sem2("act_distance")
        act_onehot = sem2("act_onehot")
        product_done = sem2("product_done")
        fixed_copied = sem2("fixed_copied")
        ids_staged = sem2("ids_staged")
        rows_landed = [[sem(f"rows_{b}{g}") for g in range(len(GROUPS))] for b in "ab"]
        turned_full = sem2("turned_full")
        turned_read = sem2("turned_read")
        feats_fixed = sem2("feats_fixed")
        gram_unit = sem2("gram_unit")
        z_dense = sem2("z_dense")
        z_copied = sem2("z_copied")
        z_merged = sem2("z_merged")
        layer1_done = sem2("layer1_done")
        h1_act = sem2("h1_act")
        h1_dve = sem2("h1_dve")
        layer2_done = sem2("layer2_done")
        h2_act = sem2("h2_act")
        h2_dve = sem2("h2_dve")
        y_done = sem("y_done")
        y_copied = sem("y_copied")
        out_stored = sem("out_stored")
        wait_carrier = sem("wait_carrier")

        def group_at(b, g):
            n = len(GROUPS) * b + g
            return n % 2, n // 2

        def slots(b, first, count):
            return feats[b][:, :].rearrange("p (s f) -> p f s", f=SLOTS)[:, first:first + count, :]

        def column_view(b, q, j, first_col):
            cols = gram[STRIP * j:STRIP * j + SLOTS, 2 * b:2 * b + 2, 0:PER_BANK * SLOTS]
            last = first_col + q + 4 * (BLOCKS_OF_STRIP[q] - 1)
            return cols.rearrange("p k (s c) -> p c k s", c=SLOTS)[:, first_col + q:last + 1:4]

        def z_view(b, q, j):
            dst = z[b][STRIP * q:STRIP * q + SLOTS, 0:BLOCKS_OF_STRIP[q], 32 * j:32 * j + 32]
            return dst.rearrange("p c (k s) -> p c k s", k=2)

        block = ctx.enter_context(nc.Block())

        @block.sync
        def _(sp):
            sp.dma_start(ids_all[:, :], ids_gathered).then_inc(ids_loaded, 16)
            sp.dma_start(const_sb[:, :], consts).then_inc(consts_loaded, 16)

            with sp.Fori(0, ROUNDS_A) as v:
                for b in range(2):
                    sp.wait_ge(lo_done[b], v + 1)
                    table = small_tables[bass.ds(2 * v + b, 1)].rearrange("o (p c) d -> (o p) c d", c=CHUNKS)
                    sp.dma_start(table_raw[0:TABLE_CUT, b], table[0:TABLE_CUT]).then_inc(table_loaded[b], 16)
                    sp.dma_start(table_raw[TABLE_CUT:, b], table[TABLE_CUT:]).then_inc(table_loaded[b], 16)
                    sp.wait_ge(dve_onehot[b], v * DVE_CHUNKS + DVE_CHUNKS)
                    sp.sem_inc(wait_carrier, 1)
                    sp.wait_ge(act_onehot[b], v * ACT_CHUNKS + ACT_CHUNKS)
                    sp.dma_start(ids_bc[:, b, :], ids_onehot[bass.ds(2 * v + b, 1), :].to_broadcast([CHUNK_ROWS, BATCH])
                                 ).then_inc(ids_bc_loaded[b], 16)

            sp.dma_start(fixed_t[:, 0, :], dense_t).then_inc(dense_loaded, 16)
            sp.dma_start(mask_sb[:, :], pair_mask).then_inc(params_loaded, 16)
            sp.dma_start(w1[:, :, :], w1_first).then_inc(w1_loaded, 16)
            sp.dma_start(w1_more[:, :, :], w1_second).then_inc(w1_loaded, 16)
            sp.dma_start(param_sb[:, :], params).then_inc(params_loaded, 16)
            sp.dma_start(w2_sb[:, :, :], w2).then_inc(params_loaded, 16)

            with sp.Fori(0, ROUNDS_B) as u:
                for b in range(2):
                    sp.wait_ge(layer1_done[b], u * NT_1 + NT_1)
                    sp.dma_start(z[b][:, :, :], dense_rows[bass.ds(2 * u + b, 1)].rearrange("o p k s -> (o p) k s")
                                 ).then_inc(z_dense[b], 16)

            sp.wait_ge(y_copied, TILES + 1)
            sp.dma_start(out, y_row[:, :]).then_inc(out_stored, 16)
            sp.wait_ge(out_stored, 16)

        @block.gpsimd
        def _(pool):
            pool.wait_ge(ids_loaded, 16)
            with pool.Fori(0, ROUNDS_B) as u:
                for b in range(2):
                    bank, before = group_at(b, len(GROUPS) - 1)
                    pool.wait_ge(turned_full[bank], u * len(GROUPS) + before + 1)
                    pool.tensor_copy(ids_now[:, b, :], ids_all[:, bass.ds((2 * u + b) * len(GATHERED), len(GATHERED))]
                                     ).then_inc(ids_staged[b], 1)
                    pool.wait_ge(ids_staged[b], u + 1)
                    pool.sem_inc(wait_carrier, 1)
                    for g, group in enumerate(GROUPS):
                        for f in group:
                            n = GATHERED.index(f)
                            pool.indirect_dma_start(
                                rows[:, b, n, :], None, tables[f],
                                bass.IndirectOffsetOnAxis(ap=ids_now[:, b, n:n + 1], axis=0),
                            ).then_inc(rows_landed[b][g], 16)

        @block.tensor
        def _(pe):
            for b in range(2):
                pe.sem_inc(product_done[b], 1)
                pe.sem_inc(turned_full[b], len(GROUPS))
                pe.sem_inc(gram_unit[b], UNITS)
                pe.sem_inc(layer1_done[b], NT_1)

            with pe.Fori(0, ROUNDS_A) as v:
                for b in range(2):
                    pe.wait_ge(fixed_copied[b], v + 1)
                    pe.wait_ge(hi_done[b], v + 1)
                    pe.wait_ge(lo_done[b], v + 2)
                    for c in range(CHUNKS):
                        if c < DVE_CHUNKS:
                            pe.wait_ge(dve_onehot[b], v * DVE_CHUNKS + DVE_CHUNKS + c + 1)
                        else:
                            pe.wait_ge(act_onehot[b], v * ACT_CHUNKS + ACT_CHUNKS + c - DVE_CHUNKS + 1)
                        pe.matmul(layer2[b][:, :], table_hi[:, b, c, :], onehot[b][:, c, :],
                                  start=(c == 0), stop=False)
                        last = pe.matmul(layer2[b][:, :], table_lo[:, b, c, :], onehot[b][:, c, :],
                                         start=False, stop=(c == CHUNKS - 1))
                    last.then_inc(product_done[b], 1)

            def transposes(u, b, groups):
                for g in groups:
                    bank, before = group_at(b, g)
                    pe.wait_ge(rows_landed[b][g], (u + 1) * 16 * len(GROUPS[g]))
                    pe.wait_ge(turned_read[bank], u * len(GROUPS) + before + 1)
                    for k, f in enumerate(GROUPS[g]):
                        last = pe.transpose(turned[bank][:, k, :], rows[:, b, GATHERED.index(f), :], identity)
                    last.then_inc(turned_full[bank], 1)

            def pairs(u, b):
                bank, before = group_at(b, len(GROUPS) - 1)
                other, before_other = group_at(b, len(GROUPS) - 2)
                pe.wait_ge(feats_fixed[b], u + 1)
                pe.wait_ge(turned_read[other], u * len(GROUPS) + before_other + 2)
                pe.wait_ge(turned_read[bank], u * len(GROUPS) + before + 2)
                for j in range(UNITS):
                    for k in range(2):
                        for i in range(PER_BANK):
                            sample = 32 * j + PER_BANK * k + i
                            vectors = feats[b][:, sample * SLOTS:(sample + 1) * SLOTS]
                            last = pe.matmul(gram[STRIP * j:STRIP * j + SLOTS, 2 * b + k, i * SLOTS:(i + 1) * SLOTS],
                                             vectors, vectors, start=True, stop=True)
                    last.then_inc(gram_unit[b], 1)

            def mlp(u, b):
                pe.wait_ge(z_merged[b], u * UNITS + UNITS)
                for n in range(NT_1):
                    for kt in range(KTILES):
                        last = pe.matmul(gram[:, n, 0:P], w1[:, kt, n * P:(n + 1) * P], z[b][:, kt, :],
                                         start=(kt == 0), stop=(kt == KTILES - 1))
                    last.then_inc(layer1_done[b], 1)
                pe.wait_ge(y_copied, 2 * u + b + 1)
                for n in range(NT_1):
                    pe.wait_ge((h1_act, h1_dve)[n % 2][b], u * (NT_1 // 2) + n // 2 + 1)
                    for m in range(NT_2):
                        last = pe.matmul(layer2[m][:, 0:P], w2_sb[:, n, m * P:(m + 1) * P], h1[:, n, :],
                                         start=(n == 0), stop=(n == NT_1 - 1))
                        if n == NT_1 - 1:
                            last.then_inc(layer2_done[b], 1)
                pe.wait_ge(h2_act[b], u + 1)
                pe.wait_ge(h2_dve[b], u + 1)
                for m in range(NT_2):
                    last = pe.matmul(layer2[0][0:1, P:2 * P], w3_sb[:, m:m + 1], h2[:, m, :],
                                     start=(m == 0), stop=(m == NT_2 - 1))
                last.then_inc(y_done, 1)

            pe.wait_ge(consts_loaded, 16)
            pe.wait_ge(params_loaded, 48)
            pe.wait_ge(w1_summed, 1)
            for b in range(2):
                pe.wait_ge(fixed_copied[b], ROUNDS_A + 1)
            with pe.Fori(0, ROUNDS_B) as u:
                transposes(u, 0, range(len(GROUPS)))
                pairs(u, 0)
                transposes(u, 1, range(EARLY_GROUPS))
                mlp(u, 0)
                transposes(u, 1, range(EARLY_GROUPS, len(GROUPS)))
                pairs(u, 1)
                mlp(u, 1)

        @block.scalar
        def _(act):
            for b in range(2):
                act.sem_inc(act_onehot[b], ACT_CHUNKS)
                act.sem_inc(fixed_copied[b], 1)
                act.sem_inc(turned_read[b], 1)
            act.sem_inc(y_copied, 1)
            act.wait_ge(consts_loaded, 16)

            def split_and_onehot(v, b):
                act.wait_ge(product_done[b], v + 1)
                act.wait_ge(table_loaded[b], v * 32 + 32)
                act.activation(table_hi[:, b], table_raw[:, b], ACT.Copy).then_inc(hi_done[b], 1)
                act.wait_ge(ids_bc_loaded[b], v * 16 + 16)
                for k in range(ACT_CHUNKS):
                    c = DVE_CHUNKS + k
                    act.wait_ge(act_onehot[b], v * ACT_CHUNKS + ACT_CHUNKS)
                    act.activation(distance[:, b, k, :], ids_bc[:, b, :], ACT.Abs, bias=minus_row_id[:, c:c + 1]
                                   ).then_inc(act_distance[b], 1)
                for k in range(ACT_CHUNKS):
                    act.wait_ge(act_distance[b], v * ACT_CHUNKS + k + 1)
                    act.activation(onehot[b][:, DVE_CHUNKS + k, :], distance[:, b, k, :], ACT.Relu, bias=1.0,
                                   scale=-1.0).then_inc(act_onehot[b], 1)

            def copy_fixed(v, b):
                act.wait_ge(product_done[b], v + 2)
                act.activation(fixed_t[:, bass.ds(2 * v + b + 1, 1), :], layer2[b][:, :].unsqueeze(1), ACT.Copy
                               ).then_inc(fixed_copied[b], 1)

            split_and_onehot(0, 0)
            with act.Fori(0, ROUNDS_A - 1) as v:
                split_and_onehot(v, 1)
                copy_fixed(v, 0)
                split_and_onehot(v + 1, 0)
                copy_fixed(v, 1)
            split_and_onehot(ROUNDS_A - 1, 1)
            copy_fixed(ROUNDS_A - 1, 0)
            copy_fixed(ROUNDS_A - 1, 1)

            def copy_turned(u, b, groups):
                for g in groups:
                    bank, before = group_at(b, g)
                    act.wait_ge(gram_unit[b], u * UNITS + UNITS)
                    act.wait_ge(turned_full[bank], (u + 1) * len(GROUPS) + before + 1)
                    first = FIXED + GATHERED.index(GROUPS[g][0])
                    act.activation(slots(b, first, len(GROUPS[g])), turned[bank][:, 0:len(GROUPS[g]), :], ACT.Copy
                                   ).then_inc(turned_read[bank], 1)

            def copy_columns(u, b):
                act.wait_ge(z_dense[b], u * 16 + 16)
                for j in range(UNITS):
                    act.wait_ge(gram_unit[b], u * UNITS + UNITS + j + 1)
                    for q in range(4):
                        act.activation(z_view(b, q, j), column_view(b, q, j, HALF), ACT.Copy
                                       ).then_inc(z_copied[b], 1)

            def mlp(u, b):
                for n in range(0, NT_1, 2):
                    act.wait_ge(layer1_done[b], u * NT_1 + NT_1 + n + 1)
                    act.activation(h1[:, n, :], gram[:, n, 0:P], ACT.Relu, bias=b1_sb[:, n:n + 1]
                                   ).then_inc(h1_act[b], 1)
                act.wait_ge(layer2_done[b], u * NT_2 + 1)
                act.activation(h2[:, 0, :], layer2[0][:, 0:P], ACT.Relu, bias=b2_sb[:, 0:1]).then_inc(h2_act[b], 1)
                act.wait_ge(y_done, 2 * u + b + 1)
                act.activation(y_row[0:1, bass.ds((2 * u + b) * P, P)], layer2[0][0:1, P:2 * P], ACT.Copy
                               ).then_inc(y_copied, 1)

            act.wait_ge(params_loaded, 48)
            with act.Fori(0, ROUNDS_B) as u:
                copy_turned(u, 0, range(len(GROUPS)))
                copy_columns(u, 0)
                copy_turned(u, 1, range(EARLY_GROUPS))
                mlp(u, 0)
                copy_turned(u, 1, range(EARLY_GROUPS, len(GROUPS)))
                copy_columns(u, 1)
                mlp(u, 1)

        @block.vector
        def _(dve):
            for b in range(2):
                dve.sem_inc(lo_done[b], 1)
                dve.sem_inc(dve_onehot[b], DVE_CHUNKS)
            dve.wait_ge(consts_loaded, 16)

            with dve.Fori(0, ROUNDS_A) as v:
                for b in range(2):
                    dve.wait_ge(product_done[b], v + 1)
                    dve.wait_ge(hi_done[b], v + 1)
                    dve.tensor_tensor(table_lo[:, b], table_raw[:, b], table_hi[:, b].bitcast(F32), ALU.subtract
                                      ).then_inc(lo_done[b], 1)
                    dve.wait_ge(ids_bc_loaded[b], v * 16 + 16)
                    for c in range(DVE_CHUNKS):
                        dve.tensor_scalar(onehot[b][:, c, :], ids_bc[:, b, :], row_id[:, c:c + 1], None, ALU.is_equal
                                          ).then_inc(dve_onehot[b], 1)

            dve.wait_ge(w1_loaded, 32)
            dve.tensor_tensor(w1[:, :, :], w1[:, :, :], w1_more[:, :, :], ALU.add).then_inc(w1_summed, 1)

            def fixed_slots(u, b):
                dve.wait_ge(gram_unit[b], u * UNITS + UNITS)
                samples = bass.ds((2 * u + b) * P, P)
                dve.tensor_copy(slots(b, 0, FIXED), fixed_t[:, :, samples]).then_inc(feats_fixed[b], 1)

            def merge_columns(u, b):
                for j in range(UNITS):
                    dve.wait_ge(z_copied[b], (u * UNITS + j + 1) * 4)
                    dve.sem_inc(wait_carrier, 1)
                    for q in range(4):
                        mask = mask_sb[STRIP * q:STRIP * q + SLOTS, 0:BLOCKS_OF_STRIP[q]]
                        mask = mask.unsqueeze(2).unsqueeze(3).to_broadcast([SLOTS, BLOCKS_OF_STRIP[q], 2, PER_BANK])
                        last = dve.copy_predicated(z_view(b, q, j), mask, column_view(b, q, j, 0))
                    last.then_inc(z_merged[b], 1)

            def mlp(u, b):
                for n in range(1, NT_1, 2):
                    dve.wait_ge(layer1_done[b], u * NT_1 + NT_1 + n + 1)
                    dve.tensor_scalar(h1[:, n, :], gram[:, n, 0:P], b1_sb[:, n:n + 1], 0.0, ALU.add, ALU.max
                                      ).then_inc(h1_dve[b], 1)
                dve.wait_ge(layer2_done[b], u * NT_2 + 2)
                dve.tensor_scalar(h2[:, 1, :], layer2[1][:, 0:P], b2_sb[:, 1:2], 0.0, ALU.add, ALU.max
                                  ).then_inc(h2_dve[b], 1)

            dve.wait_ge(params_loaded, 48)
            dve.wait_ge(dense_loaded, 16)
            for b in range(2):
                dve.wait_ge(fixed_copied[b], ROUNDS_A + 1)
            with dve.Fori(0, ROUNDS_B) as u:
                fixed_slots(u, 0)
                fixed_slots(u, 1)
                merge_columns(u, 0)
                mlp(u, 0)
                merge_columns(u, 1)
                mlp(u, 1)


def weight_rows(w1):
    first = np.zeros((KTILES * P, NEURONS_1), w1.dtype)
    second = np.zeros((KTILES * P, NEURONS_1), w1.dtype)
    for kt, p, a, b, _ in pair_places():
        f, g = min(a, b), max(a, b)
        first[kt * P + p] = w1[D + f * SLOTS - f * (f + 1) // 2 + g - f - 1]
    for d, (kt, p) in enumerate(dense_places()):
        first[kt * P + p] = w1[d]
        second[kt * P + p] = w1[D + SLOTS * (SLOTS - 1) // 2 + d]
    return [np.ascontiguousarray(x.reshape(KTILES, P, NEURONS_1).transpose(1, 0, 2)) for x in (first, second)]


def dense_row_tiles(dense):
    at = np.zeros((TILES, P, KTILES, P), dense.dtype)
    for d, (kt, p) in enumerate(dense_places()):
        at[:, p, kt, :] = dense[:, d].reshape(TILES, P)
    return at


def constants():
    row = CHUNKS * np.arange(P)[:, None] + np.arange(CHUNKS)[None, :]
    return np.concatenate([np.eye(P), row, -row], axis=1).astype(np.float32)


def mask_constant():
    mask = np.zeros((P, KTILES), np.int32)
    for kt, p, _, _, rows_a in pair_places():
        mask[p, kt] = rows_a
    return mask


def kernel(**inputs):
    import concourse.bacc as bacc
    from concourse.bass_utils import run_bass_kernel_spmd

    nc = bacc.Bacc("TRN2", target_bir_lowering=False, num_devices=1)
    arrays = {}

    def feed(name, array):
        array = np.ascontiguousarray(array)
        arrays[name] = array
        return nc.dram_tensor(name, array.shape, mybir.dt.from_np(array.dtype), kind="ExternalInput").ap()

    ids = np.asarray(inputs["ids"])
    dense = np.asarray(inputs["r_dense_output"])
    w1_first, w1_second = weight_rows(np.asarray(inputs["W_top1"]))
    by_partition = ids[:, GATHERED].reshape(TILES, P, len(GATHERED)).transpose(1, 0, 2)
    params = np.concatenate([
        np.asarray(inputs["b_top1"]).reshape(NT_1, P).T,
        np.asarray(inputs["b_top2"]).reshape(NT_2, P).T,
        np.asarray(inputs["W_top3"]).reshape(NT_2, P).T,
    ], axis=1)
    out = nc.dram_tensor("out_dram", (1, BATCH), F32, kind="ExternalOutput").ap()
    tower(
        nc,
        feed("ids_gathered_dram", by_partition.reshape(P, -1)),
        feed("ids_onehot_dram", ids[:, ONEHOT].T),
        feed("small_tables_dram", np.stack([np.asarray(inputs[f"tbl_{f}"]) for f in ONEHOT])),
        {f: feed(f"tbl_{f}_dram", np.asarray(inputs[f"tbl_{f}"])) for f in GATHERED},
        feed("dense_t_dram", dense.T),
        feed("dense_rows_dram", dense_row_tiles(dense)),
        feed("w1_first_dram", w1_first),
        feed("w1_second_dram", w1_second),
        feed("w2_dram", np.asarray(inputs["W_top2"]).reshape(NT_1, P, NEURONS_2).transpose(1, 0, 2)),
        feed("consts_dram", constants()),
        feed("params_dram", params),
        feed("pair_mask_dram", mask_constant()),
        out,
    )
    result = run_bass_kernel_spmd(nc, [arrays], core_ids=[0])
    return result.results[0]["out_dram"].reshape(BATCH, 1)
```

```python
from contextlib import ExitStack

import concourse.bass as bass
import numpy as np
from concourse import mybir

F32 = mybir.dt.float32
F32R = mybir.dt.float32r
I32 = mybir.dt.int32
ALU = mybir.AluOpType
ACT = mybir.ActivationFunctionType

P = 128
BATCH = 512
D = 128
TABLES = 26
NEURONS_1 = 512
NEURONS_2 = 256
ROWS = [125000, 1000, 12500, 1250, 1250, 1250, 12500, 1000, 1000, 12500, 12500, 1250, 1000,
        12500, 12500, 1000, 1250, 1250, 1000, 1000, 12500, 1250, 1000, 12500, 1000, 1250]

ONEHOT_ROWS = 1000
CHUNK_ROWS = 125
CHUNKS = ONEHOT_ROWS // CHUNK_ROWS
ONEHOT = [f for f in range(TABLES) if ROWS[f] == ONEHOT_ROWS]
GATHERED = [f for f in range(TABLES) if f not in ONEHOT]
BUFFERS = 3
ROUNDS = len(ONEHOT) // BUFFERS
DVE_CHUNKS = 6
ACT_CHUNKS = CHUNKS - DVE_CHUNKS
TABLE_CUT = 112

TILES = BATCH // P

FIXED = 1 + len(ONEHOT)
SLOTS = 1 + TABLES
STRIP = 32
HALF = SLOTS // 2
BLOCKS = HALF + 1
KTILES = 4
BLOCKS_OF_STRIP = [len(range(q, BLOCKS, 4)) for q in range(4)]
DENSE_STRIPS = [(slice(STRIP * q + SLOTS, STRIP * (q + 1)), slice(0, BLOCKS_OF_STRIP[q])) for q in range(4)]
DENSE_STRIPS += [(slice(STRIP * (BLOCKS % 4), P), slice(KTILES - 1, KTILES))]

GROUPS = [GATHERED[i:i + 4] for i in range(0, len(GATHERED), 4)]

UNITS = 4
PER_BANK = 16
UNIT_SAMPLES = 2 * PER_BANK
NT_1 = NEURONS_1 // P
NT_2 = NEURONS_2 // P


def feature_of_slot():
    return [0] + [1 + f for f in ONEHOT] + [1 + f for f in GATHERED]


def dense_places():
    free = []
    for kt in range(KTILES):
        for q in range(4):
            first = SLOTS if 4 * kt + q < BLOCKS else 0
            free += [(kt, STRIP * q + r) for r in range(first, STRIP)]
    return free[:D]


def pair_places():
    feature = feature_of_slot()
    places = []
    for i in range(BLOCKS):
        kt, q = divmod(i, 4)
        for r in range(SLOTS):
            if i + 1 <= r <= i + HALF:
                if i < HALF:
                    places.append((kt, STRIP * q + r, feature[r], feature[i], True))
            elif r != i:
                places.append((kt, STRIP * q + r, feature[r], feature[i + HALF], False))
    assert len({frozenset(x[2:4]) for x in places}) == len(places) == SLOTS * (SLOTS - 1) // 2
    return places


def tower(nc, ids_gathered, ids_onehot, small_tables, tables, dense_t, dense_rows, w1_first, w1_second,
          w2, consts, params, pair_mask, out):
    with ExitStack() as ctx:
        def sb(name, shape, dt=F32):
            return ctx.enter_context(nc.sbuf_tensor(name, shape, dt))

        def psum(name, shape):
            return ctx.enter_context(nc.psum_tensor(name, shape, F32))

        def sem(name):
            return ctx.enter_context(nc.semaphore(name))

        def sem3(name):
            return [sem(f"{name}_{b}") for b in range(BUFFERS)]

        ids_sb = sb("ids_sb", [P, TILES, len(GATHERED)], I32)
        rows = sb("rows", [P, TILES, len(GATHERED), D])
        table_raw = sb("table_raw", [CHUNK_ROWS, BUFFERS, CHUNKS, D])
        table_hi = sb("table_hi", [CHUNK_ROWS, BUFFERS, CHUNKS, D], F32R)
        table_lo = sb("table_lo", [CHUNK_ROWS, BUFFERS, CHUNKS, D], F32R)
        w1_more = rows[:, TILES - 1].rearrange("p g d -> p (g d)")[:, 0:KTILES * NEURONS_1].rearrange(
            "p (k n) -> p k n", k=KTILES)
        ids_bc = sb("ids_bc", [CHUNK_ROWS, BUFFERS, BATCH], I32)
        distance = sb("distance", [CHUNK_ROWS, ACT_CHUNKS, BATCH])
        onehot = sb("onehot", [CHUNK_ROWS, BUFFERS, CHUNKS, BATCH], F32R)
        fixed_t = sb("fixed_t", [P, FIXED, BATCH])
        feats = [sb(f"feats_{b}", [P, P * SLOTS]) for b in "ab"]
        z = sb("z", [P, TILES, KTILES, P])
        w1 = sb("w1", [P, KTILES, NEURONS_1])
        w2_sb = sb("w2_sb", [P, NT_1, NEURONS_2])
        const_sb = sb("const_sb", [P, P + 2 * CHUNKS])
        param_sb = sb("param_sb", [P, NT_1 + 2 * NT_2])
        mask_sb = sb("mask_sb", [P, KTILES], I32)
        h1 = sb("h1", [P, NT_1, P])
        h2 = sb("h2", [P, NT_2, P])
        y_row = sb("y_row", [1, BATCH])
        warm_up = sb("warm_up", [1, 2])

        identity = const_sb[:, 0:P]
        row_id = const_sb[0:CHUNK_ROWS, P:P + CHUNKS]
        minus_row_id = const_sb[0:CHUNK_ROWS, P + CHUNKS:P + 2 * CHUNKS]
        b1_sb = param_sb[:, 0:NT_1]
        b2_sb = param_sb[:, NT_1:NT_1 + NT_2]
        w3_sb = param_sb[:, NT_1 + NT_2:NT_1 + 2 * NT_2]

        gram = psum("gram", [P, 4, 512])
        turned = [psum(f"turned_{i}", [P, 4, P]) for i in range(2)]
        layer2 = [psum(f"layer2_{i}", [P, 512]) for i in range(2)]

        ids_loaded = sem("ids_loaded")
        consts_loaded = sem("consts_loaded")
        dense_loaded = sem("dense_loaded")
        mask_loaded = sem("mask_loaded")
        params_loaded = sem("params_loaded")
        w1_loaded = sem("w1_loaded")
        w2_loaded = sem("w2_loaded")
        z_dense = sem("z_dense")
        w1_more_cleared = sem("w1_more_cleared")
        w1_summed = sem("w1_summed")
        warm_up_set = sem("warm_up_set")
        table_loaded = sem3("table_loaded")
        ids_bc_loaded = sem3("ids_bc_loaded")
        hi_done = sem3("hi_done")
        lo_done = sem3("lo_done")
        dve_onehot = sem3("dve_onehot")
        act_distance = sem3("act_distance")
        act_onehot = sem3("act_onehot")
        product_done = sem3("product_done")
        product_copied = sem3("product_copied")
        rows_landed = [[sem(f"rows_{t}_{g}") for g in range(len(GROUPS))] for t in range(TILES)]
        turned_full = sem("turned_full")
        turned_read = sem("turned_read")
        feats_fixed = sem("feats_fixed")
        gram_unit = sem("gram_unit")
        z_copied = sem("z_copied")
        z_merged = sem("z_merged")
        layer1_done = sem("layer1_done")
        h1_act = sem("h1_act")
        h1_dve = sem("h1_dve")
        layer2_done = sem("layer2_done")
        h2_act = sem("h2_act")
        h2_dve = sem("h2_dve")
        y_done = sem("y_done")
        y_copied = sem("y_copied")
        out_stored = sem("out_stored")
        wait_carrier = sem("wait_carrier")

        def slots(t, first, count):
            return feats[t % 2][:, :].rearrange("p (s f) -> p f s", f=SLOTS)[:, first:first + count, :]

        def column_view(t, q, j, first_col):
            b = t % 2
            cols = gram[STRIP * j:STRIP * j + SLOTS, 2 * b:2 * b + 2, 0:PER_BANK * SLOTS]
            last = first_col + q + 4 * (BLOCKS_OF_STRIP[q] - 1)
            return cols.rearrange("p k (s c) -> p c k s", c=SLOTS)[:, first_col + q:last + 1:4]

        def z_view(t, q, j):
            dst = z[STRIP * q:STRIP * q + SLOTS, t, 0:BLOCKS_OF_STRIP[q], UNIT_SAMPLES * j:UNIT_SAMPLES * (j + 1)]
            return dst.rearrange("p c (k s) -> p c k s", k=2)

        def layer1_out(t, n):
            return gram[:, 2 * (t % 2) + n // 2, (n % 2) * P:(n % 2 + 1) * P]

        block = ctx.enter_context(nc.Block())

        @block.sync
        def _(sp):
            sp.dma_start(ids_sb[:, :, :], ids_gathered).then_inc(ids_loaded, 16)

            def load_table(v, b):
                table = small_tables[bass.ds(BUFFERS * v + b, 1)].rearrange("o (p c) d -> (o p) c d", c=CHUNKS)
                ids = ids_onehot[bass.ds(BUFFERS * v + b, 1), :].to_broadcast([CHUNK_ROWS, BATCH])
                sp.wait_ge(lo_done[b], v + 1)
                sp.dma_start(table_raw[0:TABLE_CUT, b], table[0:TABLE_CUT]).then_inc(table_loaded[b], 16)
                sp.dma_start(table_raw[TABLE_CUT:, b], table[TABLE_CUT:]).then_inc(table_loaded[b], 16)
                sp.wait_ge(dve_onehot[b], v * DVE_CHUNKS + DVE_CHUNKS)
                sp.sem_inc(wait_carrier, 1)
                sp.wait_ge(act_onehot[b], v * ACT_CHUNKS + ACT_CHUNKS)
                sp.dma_start(ids_bc[:, b, :], ids).then_inc(ids_bc_loaded[b], 16)

            sp.dma_start(const_sb[:, :], consts).then_inc(consts_loaded, 16)
            load_table(0, 0)
            load_table(0, 1)
            load_table(0, 2)
            with sp.Fori(1, ROUNDS) as v:
                for b in range(BUFFERS):
                    load_table(v, b)

            sp.dma_start(w1[:, :, :], w1_first).then_inc(w1_loaded, 16)
            sp.wait_ge(w1_more_cleared, 1)
            for strip, kts in DENSE_STRIPS:
                sp.dma_start(w1_more[strip, kts, :], w1_second[strip, kts, :]).then_inc(w1_loaded, 16)
            sp.dma_start(fixed_t[:, 0, :], dense_t).then_inc(dense_loaded, 16)
            sp.dma_start(mask_sb[:, :], pair_mask).then_inc(mask_loaded, 16)
            for strip, kts in DENSE_STRIPS:
                sp.dma_start(z[strip, :, kts, :], dense_rows[strip, :, kts, :]).then_inc(z_dense, 16)
            sp.dma_start(param_sb[:, :], params).then_inc(params_loaded, 16)
            sp.dma_start(w2_sb[:, :, :], w2).then_inc(w2_loaded, 16)

            sp.wait_ge(y_copied, TILES)
            sp.dma_start(out, y_row[:, :]).then_inc(out_stored, 16)
            sp.wait_ge(out_stored, 16)

        @block.gpsimd
        def _(pool):
            pool.wait_ge(ids_loaded, 16)
            for t in range(TILES):
                if t == TILES - 1:
                    pool.wait_ge(w1_summed, 1)
                for g, group in enumerate(GROUPS):
                    for f in group:
                        n = GATHERED.index(f)
                        pool.indirect_dma_start(
                            rows[:, t, n, :], None, tables[f],
                            bass.IndirectOffsetOnAxis(ap=ids_sb[:, t, n:n + 1], axis=0),
                        ).then_inc(rows_landed[t][g], 16)


        @block.tensor
        def _(pe):
            for b in range(BUFFERS):
                pe.sem_inc(product_done[b], 1)

            def product(v, b):
                pe.wait_ge(product_copied[b], v + 1)
                pe.wait_ge(hi_done[b], v + 1)
                for c in range(CHUNKS):
                    if c < DVE_CHUNKS:
                        pe.wait_ge(dve_onehot[b], v * DVE_CHUNKS + DVE_CHUNKS + c + 1)
                    else:
                        pe.wait_ge(act_onehot[b], v * ACT_CHUNKS + ACT_CHUNKS + c - DVE_CHUNKS + 1)
                    pe.matmul(gram[:, b, :], table_hi[:, b, c, :], onehot[:, b, c, :],
                              start=(c == 0), stop=False)
                pe.wait_ge(lo_done[b], v + 2)
                for c in range(CHUNKS):
                    last = pe.matmul(gram[:, b, :], table_lo[:, b, c, :], onehot[:, b, c, :],
                                     start=False, stop=(c == CHUNKS - 1))
                last.then_inc(product_done[b], 1)

            def transposes(t, groups):
                for g in groups:
                    n = t * len(GROUPS) + g
                    pe.wait_ge(rows_landed[t][g], 16 * len(GROUPS[g]))
                    if n >= 2:
                        pe.wait_ge(turned_read, n - 1)
                    for k, f in enumerate(GROUPS[g]):
                        last = pe.transpose(turned[n % 2][:, k, :], rows[:, t, GATHERED.index(f), :], identity)
                    last.then_inc(turned_full, 1)

            def pairs(t, units=range(UNITS), interleaved=False):
                pe.wait_ge(feats_fixed, (4 if t < 2 else t + 3))
                pe.wait_ge(turned_read, (t + 1) * len(GROUPS))
                if t < 2:
                    for b in range(BUFFERS):
                        pe.wait_ge(product_copied[b], ROUNDS + 1)
                else:
                    pe.wait_ge(h1_act, (t - 1) * NT_1 // 2)
                    pe.wait_ge(h1_dve, (t - 1) * NT_1 // 2)
                for group in ([units] if interleaved else [[j] for j in units]):
                    for i in range(UNIT_SAMPLES):
                        k, column = divmod(i, PER_BANK)
                        for j in group:
                            sample = UNIT_SAMPLES * j + i
                            vectors = feats[t % 2][:, sample * SLOTS:(sample + 1) * SLOTS]
                            last = pe.matmul(
                                gram[STRIP * j:STRIP * j + SLOTS, 2 * (t % 2) + k,
                                     column * SLOTS:(column + 1) * SLOTS],
                                vectors, vectors, start=True, stop=True)
                            if i == UNIT_SAMPLES - 1:
                                last.then_inc(gram_unit, 1)

            def first_layer(t, ns=range(NT_1)):
                pe.wait_ge(z_merged, (t + 1) * UNITS)
                if t == 0:
                    pe.wait_ge(w1_summed, 1)
                for n in ns:
                    for kt in range(KTILES):
                        last = pe.matmul(layer1_out(t, n), w1[:, kt, n * P:(n + 1) * P], z[:, t, kt, :],
                                         start=(kt == 0), stop=(kt == KTILES - 1))
                    if n % 2:
                        last.then_inc(layer1_done, 1)

            def second_layer(t, ns=range(NT_1)):
                if t == 0:
                    pe.wait_ge(w2_loaded, 16)
                else:
                    pe.wait_ge(y_copied, t)
                for n in ns:
                    pe.wait_ge((h1_act, h1_dve)[n % 2], t * (NT_1 // 2) + n // 2 + 1)
                    for m in range(NT_2):
                        last = pe.matmul(layer2[m][:, 0:P], w2_sb[:, n, m * P:(m + 1) * P], h1[:, n, :],
                                         start=(n == 0), stop=(n == NT_1 - 1))
                        if n == NT_1 - 1:
                            last.then_inc(layer2_done, 1)

            def third_layer(t):
                pe.wait_ge(h2_act, t + 1)
                pe.wait_ge(h2_dve, t + 1)
                for m in range(NT_2):
                    last = pe.matmul(layer2[0][0:1, P:2 * P], w3_sb[:, m:m + 1], h2[:, m, :],
                                     start=(m == 0), stop=(m == NT_2 - 1))
                last.then_inc(y_done, 1)

            with pe.Fori(0, ROUNDS - 1) as v:
                for b in range(BUFFERS):
                    product(v, b)
            pe.wait_ge(consts_loaded, 16)
            transposes(0, [0, 1])
            product(ROUNDS - 1, 0)
            transposes(0, [2, 3])
            product(ROUNDS - 1, 1)
            transposes(0, [4])
            product(ROUNDS - 1, 2)
            transposes(1, [0, 1, 2])
            pairs(0, [0])
            transposes(1, [3, 4])
            pairs(0, [1, 2, 3])
            pairs(1)
            first_layer(0)
            transposes(2, [0, 1])
            second_layer(0)
            transposes(2, [2, 3])
            third_layer(0)
            transposes(2, [4])
            first_layer(1)
            pairs(2, [0, 1], interleaved=True)
            second_layer(1, [0, 1])
            pairs(2, [2, 3])
            second_layer(1, [2, 3])
            transposes(3, [0, 1])
            first_layer(2)
            third_layer(1)
            transposes(3, [2, 3, 4])
            pairs(3)
            second_layer(2)
            first_layer(3, [0, 1])
            third_layer(2)
            first_layer(3, [2, 3])
            second_layer(3)
            third_layer(3)

        @block.scalar
        def _(act):
            for b in range(BUFFERS):
                act.sem_inc(act_onehot[b], ACT_CHUNKS)
                act.sem_inc(product_copied[b], 1)
            act.wait_ge(warm_up_set, 1)
            act.activation(warm_up[0:1, 1:2], warm_up[0:1, 0:1], ACT.Copy)

            def split_and_onehot(v, b):
                act.wait_ge(product_done[b], v + 1)
                act.wait_ge(table_loaded[b], v * 32 + 32)
                act.activation(table_hi[:, b], table_raw[:, b], ACT.Copy).then_inc(hi_done[b], 1)
                act.wait_ge(consts_loaded, 16)
                act.wait_ge(ids_bc_loaded[b], v * 16 + 16)
                last_v, last_b = (v, b - 1) if b else (v - 1, BUFFERS - 1)
                act.wait_ge(act_onehot[last_b], last_v * ACT_CHUNKS + 2 * ACT_CHUNKS)
                for k in range(ACT_CHUNKS):
                    c = DVE_CHUNKS + k
                    act.activation(distance[:, k, :], ids_bc[:, b, :], ACT.Abs, bias=minus_row_id[:, c:c + 1]
                                   ).then_inc(act_distance[b], 1)
                for k in range(ACT_CHUNKS):
                    act.wait_ge(act_distance[b], v * ACT_CHUNKS + k + 1)
                    act.activation(onehot[:, b, DVE_CHUNKS + k, :], distance[:, k, :], ACT.Relu, bias=1.0,
                                   scale=-1.0).then_inc(act_onehot[b], 1)

            def copy_product(v, b):
                act.wait_ge(product_done[b], v + 2)
                act.activation(fixed_t[:, bass.ds(BUFFERS * v + b + 1, 1), :], gram[:, b, :].unsqueeze(1), ACT.Copy
                               ).then_inc(product_copied[b], 1)

            def copy_turned(t, groups):
                for g in groups:
                    n = t * len(GROUPS) + g
                    if t >= 2:
                        act.wait_ge(gram_unit, (t - 1) * UNITS)
                    act.wait_ge(turned_full, n + 1)
                    first = FIXED + GATHERED.index(GROUPS[g][0])
                    act.activation(slots(t, first, len(GROUPS[g])), turned[n % 2][:, 0:len(GROUPS[g]), :], ACT.Copy
                                   ).then_inc(turned_read, 1)

            def copy_columns(t, units=range(UNITS)):
                for j in units:
                    act.wait_ge(gram_unit, t * UNITS + j + 1)
                    for q in range(4):
                        last = act.activation(z_view(t, q, j), column_view(t, q, j, HALF), ACT.Copy)
                    last.then_inc(z_copied, 1)

            def relu_1(t, ns=range(0, NT_1, 2)):
                for n in ns:
                    act.wait_ge(layer1_done, t * NT_1 // 2 + n // 2 + 1)
                    act.activation(h1[:, n, :], layer1_out(t, n), ACT.Relu, bias=b1_sb[:, n:n + 1]
                                   ).then_inc(h1_act, 1)

            def relu_2(t):
                act.wait_ge(layer2_done, t * NT_2 + 1)
                act.activation(h2[:, 0, :], layer2[0][:, 0:P], ACT.Relu, bias=b2_sb[:, 0:1]).then_inc(h2_act, 1)

            def copy_y(t):
                act.wait_ge(y_done, t + 1)
                act.activation(y_row[0:1, t * P:(t + 1) * P], layer2[0][0:1, P:2 * P], ACT.Copy).then_inc(y_copied, 1)

            split_and_onehot(0, 0)
            with act.Fori(0, ROUNDS - 1) as v:
                split_and_onehot(v, 1)
                copy_product(v, 0)
                split_and_onehot(v, 2)
                copy_product(v, 1)
                split_and_onehot(v + 1, 0)
                copy_product(v, 2)
            copy_turned(0, [0, 1])
            split_and_onehot(ROUNDS - 1, 1)
            copy_product(ROUNDS - 1, 0)
            copy_turned(0, [2, 3])
            split_and_onehot(ROUNDS - 1, 2)
            copy_product(ROUNDS - 1, 1)
            copy_turned(0, [4])
            copy_product(ROUNDS - 1, 2)
            copy_turned(1, [0, 1, 2])
            act.wait_ge(z_dense, 16 * len(DENSE_STRIPS))
            act.wait_ge(params_loaded, 16)
            copy_columns(0, [0])
            copy_turned(1, [3, 4])
            copy_columns(0, [1, 2, 3])
            copy_columns(1)
            relu_1(0)
            copy_turned(2, [0, 1])
            relu_2(0)
            copy_turned(2, [2, 3])
            copy_y(0)
            copy_turned(2, [4])
            relu_1(1)
            copy_columns(2)
            relu_2(1)
            copy_turned(3, [0, 1])
            relu_1(2)
            copy_y(1)
            copy_turned(3, [2, 3, 4])
            copy_columns(3)
            relu_2(2)
            relu_1(3, [0])
            copy_y(2)
            relu_1(3, [2])
            relu_2(3)
            copy_y(3)

        @block.vector
        def _(dve):
            dve.memset(warm_up[:, :], 0.0).then_inc(warm_up_set, 1)
            for b in range(BUFFERS):
                dve.sem_inc(lo_done[b], 1)
                dve.sem_inc(dve_onehot[b], DVE_CHUNKS)
            dve.memset(w1_more, 0.0).then_inc(w1_more_cleared, 1)
            dve.wait_ge(consts_loaded, 16)

            def split_and_onehot(v, b):
                dve.wait_ge(product_done[b], v + 1)
                dve.wait_ge(ids_bc_loaded[b], v * 16 + 16)
                for c in range(DVE_CHUNKS):
                    dve.tensor_scalar(onehot[:, b, c, :], ids_bc[:, b, :], row_id[:, c:c + 1], None, ALU.is_equal
                                      ).then_inc(dve_onehot[b], 1)
                dve.wait_ge(hi_done[b], v + 1)
                dve.tensor_tensor(table_lo[:, b], table_raw[:, b], table_hi[:, b].bitcast(F32), ALU.subtract
                                  ).then_inc(lo_done[b], 1)

            def fixed_slots(t, first, count):
                if t >= 2:
                    dve.wait_ge(gram_unit, (t - 1) * UNITS)
                dve.tensor_copy(slots(t, first, count), fixed_t[:, first:first + count, t * P:(t + 1) * P]
                                ).then_inc(feats_fixed, 1)

            def merge_columns(t):
                for j in range(UNITS):
                    dve.wait_ge(z_copied, t * UNITS + j + 1)
                    for q in range(4):
                        mask = mask_sb[STRIP * q:STRIP * q + SLOTS, 0:BLOCKS_OF_STRIP[q]]
                        mask = mask.unsqueeze(2).unsqueeze(3).to_broadcast([SLOTS, BLOCKS_OF_STRIP[q], 2, PER_BANK])
                        last = dve.copy_predicated(z_view(t, q, j), mask, column_view(t, q, j, 0))
                    last.then_inc(z_merged, 1)

            def relu_1(t):
                for n in range(1, NT_1, 2):
                    dve.wait_ge(h1_act, t * NT_1 // 2 + n // 2 + 1)
                    dve.tensor_scalar(h1[:, n, :], layer1_out(t, n), b1_sb[:, n:n + 1], 0.0, ALU.add, ALU.max
                                      ).then_inc(h1_dve, 1)

            def relu_2(t):
                dve.wait_ge(layer2_done, t * NT_2 + 2)
                dve.tensor_scalar(h2[:, 1, :], layer2[1][:, 0:P], b2_sb[:, 1:2], 0.0, ALU.add, ALU.max
                                  ).then_inc(h2_dve, 1)

            with dve.Fori(0, ROUNDS) as v:
                for b in range(BUFFERS):
                    split_and_onehot(v, b)

            dve.wait_ge(w1_loaded, 16 * (1 + len(DENSE_STRIPS)))
            dve.tensor_tensor(w1[:, :, :], w1[:, :, :], w1_more, ALU.add).then_inc(w1_summed, 1)
            dve.wait_ge(dense_loaded, 16)
            for b in range(BUFFERS):
                dve.wait_ge(product_copied[b], ROUNDS + (b < BUFFERS - 1))
            fixed_slots(0, 0, FIXED - 1)
            fixed_slots(1, 0, FIXED - 1)
            dve.wait_ge(product_copied[BUFFERS - 1], ROUNDS + 1)
            fixed_slots(0, FIXED - 1, 1)
            fixed_slots(1, FIXED - 1, 1)
            dve.wait_ge(mask_loaded, 16)
            dve.wait_ge(params_loaded, 16)
            merge_columns(0)
            fixed_slots(2, 0, FIXED)
            merge_columns(1)
            fixed_slots(3, 0, FIXED)
            relu_1(0)
            relu_2(0)
            relu_1(1)
            merge_columns(2)
            relu_2(1)
            relu_1(2)
            merge_columns(3)
            relu_2(2)
            relu_1(3)
            relu_2(3)


def weight_rows(w1):
    first = np.zeros((KTILES * P, NEURONS_1), w1.dtype)
    second = np.zeros((KTILES * P, NEURONS_1), w1.dtype)
    for kt, p, a, b, _ in pair_places():
        f, g = min(a, b), max(a, b)
        first[kt * P + p] = w1[D + f * SLOTS - f * (f + 1) // 2 + g - f - 1]
    for d, (kt, p) in enumerate(dense_places()):
        first[kt * P + p] = w1[d]
        second[kt * P + p] = w1[D + SLOTS * (SLOTS - 1) // 2 + d]
    return [np.ascontiguousarray(x.reshape(KTILES, P, NEURONS_1).transpose(1, 0, 2)) for x in (first, second)]


def dense_row_tiles(dense):
    at = np.zeros((P, TILES, KTILES, P), dense.dtype)
    for d, (kt, p) in enumerate(dense_places()):
        at[p, :, kt, :] = dense[:, d].reshape(TILES, P)
    return at


def constants():
    row = CHUNKS * np.arange(P)[:, None] + np.arange(CHUNKS)[None, :]
    return np.concatenate([np.eye(P), row, -row], axis=1).astype(np.float32)


def mask_constant():
    mask = np.zeros((P, KTILES), np.int32)
    for kt, p, _, _, rows_a in pair_places():
        mask[p, kt] = rows_a
    return mask


def kernel(**inputs):
    import concourse.bacc as bacc
    from concourse.bass_utils import run_bass_kernel_spmd

    nc = bacc.Bacc("TRN2", target_bir_lowering=False, num_devices=1)
    arrays = {}

    def feed(name, array):
        array = np.ascontiguousarray(array)
        arrays[name] = array
        return nc.dram_tensor(name, array.shape, mybir.dt.from_np(array.dtype), kind="ExternalInput").ap()

    ids = np.asarray(inputs["ids"])
    dense = np.asarray(inputs["r_dense_output"])
    w1_first, w1_second = weight_rows(np.asarray(inputs["W_top1"]))
    by_partition = ids[:, GATHERED].reshape(TILES, P, len(GATHERED)).transpose(1, 0, 2)
    params = np.concatenate([
        np.asarray(inputs["b_top1"]).reshape(NT_1, P).T,
        np.asarray(inputs["b_top2"]).reshape(NT_2, P).T,
        np.asarray(inputs["W_top3"]).reshape(NT_2, P).T,
    ], axis=1)
    out = nc.dram_tensor("out_dram", (1, BATCH), F32, kind="ExternalOutput").ap()
    tower(
        nc,
        feed("ids_gathered_dram", by_partition),
        feed("ids_onehot_dram", ids[:, ONEHOT].T),
        feed("small_tables_dram", np.stack([np.asarray(inputs[f"tbl_{f}"]) for f in ONEHOT])),
        {f: feed(f"tbl_{f}_dram", np.asarray(inputs[f"tbl_{f}"])) for f in GATHERED},
        feed("dense_t_dram", dense.T),
        feed("dense_rows_dram", dense_row_tiles(dense)),
        feed("w1_first_dram", w1_first),
        feed("w1_second_dram", w1_second),
        feed("w2_dram", np.asarray(inputs["W_top2"]).reshape(NT_1, P, NEURONS_2).transpose(1, 0, 2)),
        feed("consts_dram", constants()),
        feed("params_dram", params),
        feed("pair_mask_dram", mask_constant()),
        out,
    )
    result = run_bass_kernel_spmd(nc, [arrays], core_ids=[0])
    return result.results[0]["out_dram"].reshape(BATCH, 1)
```
